# Optimizing a Trainium2 kernel written in Bass

```python
import numpy as np
import jax
import jax.numpy as jnp

def _softmax(x, axis=-1):
    return jax.nn.softmax(x, axis=axis)

def _gelu(x):
    return jax.nn.gelu(x, approximate=True)

def _silu(x):
    return jax.nn.silu(x)

def _sigmoid(x):
    return jax.nn.sigmoid(x)

def _layernorm(x, axis=-1, eps=1e-05):
    m = jnp.mean(x, axis=axis, keepdims=True)
    v = jnp.var(x, axis=axis, keepdims=True)
    return (x - m) / jnp.sqrt(v + eps)

def _scatter_add(tgt, idx, src, axis=0):
    return tgt.at[idx].add(src)

def _segment_sum(src, seg, n):
    return jax.ops.segment_sum(src, seg, n)
kernel_name = 'mk_cond_resid_d1_seqx_r2_fb1bed'

def setup_inputs(seed: int=0):
    np.random.seed(seed)
    _w = jnp.asarray

    def _rec_inputs():
        import jax
        import jax.numpy as jnp
        _rk = jax.random.key(seed)
        x = -0.000125 + 0.9999 * jax.random.normal(jax.random.fold_in(_rk, 1), (64, 128, 512), jnp.float32)
        _lenS = 128 - jax.random.randint(jax.random.fold_in(_rk, 7), (64,), 0, max(1, 128 // 4) + 1, jnp.int32)
        _lenS2 = 128 - jax.random.randint(jax.random.fold_in(_rk, 8), (64,), 0, max(1, 128 // 4) + 1, jnp.int32)
        cond_1024 = -0.00493535 + 1.00056 * jax.random.normal(jax.random.fold_in(_rk, 11), (64, 512), jnp.float32)
        return (x, cond_1024)
    x, cond_1024 = _rec_inputs()

    def _L0_cond_setup():
        import jax, jax.numpy as jnp
        import numpy as np
        INPUT_DIM = 512
        HIDDEN_DIM = 512
        CHUNK_SIZE = 4

        def _linear_params(key, fan_in, fan_out):
            kw, kb = jax.random.split(key)
            bound = 1.0 / np.sqrt(fan_in)
            W = jax.random.uniform(kw, (fan_in, fan_out), jnp.float32, -bound, bound)
            b = jax.random.uniform(kb, (fan_out,), jnp.float32, -bound, bound)
            return (W, b)

        def _gru_forward(x, h0, Wz, bz, Wr, br, Wh, bh, Wp, bp):
            B, T, D = x.shape
            t = jnp.arange(T)
            do_prop = ((t + 1) % CHUNK_SIZE == 0) & (t < T - 1)
            xs = jnp.transpose(x, (1, 0, 2))

            def step(h, inp):
                x_t, prop = inp
                comb = jnp.concatenate([x_t, h], axis=-1)
                z = jax.nn.sigmoid(comb @ Wz + bz)
                r = jax.nn.sigmoid(comb @ Wr + br)
                comb2 = jnp.concatenate([x_t, r * h], axis=-1)
                h_cand = jnp.tanh(comb2 @ Wh + bh)
                h_new = (1.0 - z) * h + z * h_cand
                h_next = jnp.where(prop, jnp.tanh(h_new @ Wp + bp), h_new)
                return (h_next, h_new)
            _, ys = jax.lax.scan(step, h0, (xs, do_prop))
            return jnp.transpose(ys, (1, 0, 2))
        key = jax.random.key(seed)
        ks = jax.random.split(key, 6)
        x = jax.random.normal(ks[0], (64, 256, INPUT_DIM), jnp.float32)
        h0 = jax.random.normal(ks[1], (64, HIDDEN_DIM), jnp.float32)
        Wz, bz = _linear_params(ks[2], INPUT_DIM + HIDDEN_DIM, HIDDEN_DIM)
        Wr, br = _linear_params(ks[3], INPUT_DIM + HIDDEN_DIM, HIDDEN_DIM)
        Wh, bh = _linear_params(ks[4], INPUT_DIM + HIDDEN_DIM, HIDDEN_DIM)
        Wp, bp = _linear_params(ks[5], HIDDEN_DIM, HIDDEN_DIM)
        return {'x': x, 'h0': h0, 'Wz': Wz, 'bz': bz, 'Wr': Wr, 'br': br, 'Wh': Wh, 'bh': bh, 'Wp': Wp, 'bp': bp}
    _L0_cond_all = _L0_cond_setup()
    _L0_cond_in = {k: v for k, v in _L0_cond_all.items() if k in ('Wz', 'bz', 'Wr', 'br', 'Wh', 'bh', 'Wp', 'bp')}
    del _L0_cond_all
    return {'x': x, 'cond_1024': cond_1024, 'L0_cond_Wz': _L0_cond_in['Wz'], 'L0_cond_bz': _L0_cond_in['bz'], 'L0_cond_Wr': _L0_cond_in['Wr'], 'L0_cond_br': _L0_cond_in['br'], 'L0_cond_Wh': _L0_cond_in['Wh'], 'L0_cond_bh': _L0_cond_in['bh'], 'L0_cond_Wp': _L0_cond_in['Wp'], 'L0_cond_bp': _L0_cond_in['bp']}

def reference(x, cond_1024, L0_cond_Wz, L0_cond_bz, L0_cond_Wr, L0_cond_br, L0_cond_Wh, L0_cond_bh, L0_cond_Wp, L0_cond_bp):
    import jax
    import jax.numpy as jnp

    def _L0_cond_ref(x, h0, Wz, bz, Wr, br, Wh, bh, Wp, bp):
        import jax, jax.numpy as jnp
        import numpy as np
        INPUT_DIM = 512
        HIDDEN_DIM = 512
        CHUNK_SIZE = 4

        def _linear_params(key, fan_in, fan_out):
            kw, kb = jax.random.split(key)
            bound = 1.0 / np.sqrt(fan_in)
            W = jax.random.uniform(kw, (fan_in, fan_out), jnp.float32, -bound, bound)
            b = jax.random.uniform(kb, (fan_out,), jnp.float32, -bound, bound)
            return (W, b)

        def _gru_forward(x, h0, Wz, bz, Wr, br, Wh, bh, Wp, bp):
            B, T, D = x.shape
            t = jnp.arange(T)
            do_prop = ((t + 1) % CHUNK_SIZE == 0) & (t < T - 1)
            xs = jnp.transpose(x, (1, 0, 2))

            def step(h, inp):
                x_t, prop = inp
                comb = jnp.concatenate([x_t, h], axis=-1)
                z = jax.nn.sigmoid(comb @ Wz + bz)
                r = jax.nn.sigmoid(comb @ Wr + br)
                comb2 = jnp.concatenate([x_t, r * h], axis=-1)
                h_cand = jnp.tanh(comb2 @ Wh + bh)
                h_new = (1.0 - z) * h + z * h_cand
                h_next = jnp.where(prop, jnp.tanh(h_new @ Wp + bp), h_new)
                return (h_next, h_new)
            _, ys = jax.lax.scan(step, h0, (xs, do_prop))
            return jnp.transpose(ys, (1, 0, 2))
        return _gru_forward(x, h0, Wz, bz, Wr, br, Wh, bh, Wp, bp)
    x = x + _L0_cond_ref(x, cond_1024, L0_cond_Wz, L0_cond_bz, L0_cond_Wr, L0_cond_br, L0_cond_Wh, L0_cond_bh, L0_cond_Wp, L0_cond_bp)
    return x

_drawn_inputs = setup_inputs


def setup_inputs(seed=0):
    import zlib

    import numpy as np

    out = dict(_drawn_inputs(seed))
    spreads = {}
    factors = {'L0_cond_bz': 28.431,
     'L0_cond_Wr': 23.515,
     'L0_cond_br': 64.0,
     'L0_cond_bh': 4.394,
     'L0_cond_bp': 7.723}
    for name, (base, spread) in spreads.items():
        noise = np.random.default_rng([zlib.crc32(name.encode()), seed]).standard_normal(out[name].shape)
        drawn = base * np.exp(spread * noise) if base else spread * noise
        out[name] = jnp.asarray(drawn.astype(out[name].dtype))
    for name, factor in factors.items():
        out[name] = (out[name] * factor).astype(out[name].dtype)
    return out
```

```python
from contextlib import ExitStack

import concourse.bass as bass
from concourse import mybir

ALU = mybir.AluOpType
ACT = mybir.ActivationFunctionType
F32 = mybir.dt.float32
F32R = mybir.dt.float32r
F16 = mybir.dt.float16
U32 = mybir.dt.uint32
AX_X = mybir.AxisListType.X
ABS_MAX = bass.bass_isa.ReduceOp.absmax

P = 128
CHUNK = 4
RING = 3
X_BANKS = 4
R, Z, C, PROP = range(4)
GATES = 3

EXP_MASK = 0x7F800000
TOP = 14
TINY = 2.0**-80

FILL = [(8, 22, 0), (8, 22, 0), (8, 22, 0), (6, 24, 24)]


def gru_kernel(nc, x, h0, wz, wr, wh, wp, biases, out):
    BLOCKS, _, KC, _, B = x.shape
    H = wp.shape[0]
    D = wr.shape[0] - H
    assert D == H == KC * P
    N = CHUNK * B
    GROUPS = GATES * KC
    PER_GROUP = 3 * KC
    assert sum(map(sum, FILL)) == GROUPS * PER_GROUP
    LOOPS = (BLOCKS - 2) // RING
    PEELED = BLOCKS - LOOPS * RING
    assert PEELED == 2

    rows = "(k p) n -> p k n"
    w_in = {R: wr[0:D, :].rearrange(rows, p=P), Z: wz[0:D, :].rearrange(rows, p=P), C: wh[0:D, :].rearrange(rows, p=P)}
    w_rec = {R: wr[D:, :].rearrange(rows, p=P), Z: wz[D:, :].rearrange(rows, p=P),
             C: wh[D:, :].rearrange(rows, p=P), PROP: wp.rearrange(rows, p=P)}

    with ExitStack() as ctx:
        def sb(name, shape, dt=F32):
            return ctx.enter_context(nc.sbuf_tensor(name, shape, dt))

        def sem(name):
            return ctx.enter_context(nc.semaphore(name))

        win_hi = [sb(f"win_hi{g}", [P, KC, H], F32R) for g in range(GATES)]
        win_lo = [sb(f"win_lo{g}", [P, KC, H], F32R) for g in range(GATES)]
        wrec_hi = [sb(f"wrec_hi{g}", [P, KC, H], F16) for g in range(4)]
        wrec_lo = [sb(f"wrec_lo{g}", [P, KC, H], F16) for g in range(4)]
        bias = sb("bias", [P, 4, KC])
        prop_bias = sb("prop_bias", [P, KC, B])

        x_blk = [sb(f"x_blk{n}", [P, KC, CHUNK, B]) for n in range(RING)]
        x_hi = [sb(f"x_hi{n}", [P, KC, N], F32R) for n in range(RING)]
        x_lo = [sb(f"x_lo{n}", [P, KC, N], F32R) for n in range(RING)]
        x_part = [sb(f"x_part{n}", [P, GATES, KC, CHUNK, B]) for n in range(RING)]
        stage = [sb("stage0", [P, KC, H])[:]] + [
            x_part[n][:, 0:2].rearrange("p g j s b -> p (g j s b)").rearrange("p (k n) -> p k n", k=KC) for n in (1, 2)]
        out_blk = [sb(f"out_blk{n}", [P, KC, CHUNK, B]) for n in range(RING)]

        h_even_odd = [sb("h_even", [P, KC, B]), sb("h_odd", [P, KC, B])]
        h_prop = sb("h_prop", [P, KC, B])
        h_split = sb("h_split", [P, KC, 2, B], F16)
        q_split = sb("q_split", [P, KC, 2, B], F16)
        p_split = sb("p_split", [P, KC, 2, B], F16)
        part = [sb(f"part{g}", [P, KC, B]) for g in range(4)]
        gate = [sb(f"gate{g}", [P, KC, B]) for g in range(4)]
        q_full = sb("q_full", [P, KC, B])
        keep = sb("keep", [P, KC, B])
        new = sb("new", [P, KC, B])
        unscaled = sb("unscaled", [P, KC, B])
        ones = new
        h_unscale_row = sb("h_unscale_row", [P, KC, B])

        HS = 4
        mag = sb("mag", [P, 5])
        mag_all = sb("mag_all", [P, 5])
        pow2 = sb("pow2", [P, 5])
        inv_pow2 = sb("inv_pow2", [P, 5])
        scale = sb("scale", [P, 5])
        unscale = sb("unscale", [P, 5])
        h_scale, h_unscale = scale[:, HS:HS + 1], unscale[:, HS:HS + 1]

        acc = [ctx.enter_context(nc.psum_tensor(f"acc{g}", [P, KC, 2, B], F32)) for g in range(4)]
        x_acc = [ctx.enter_context(nc.psum_tensor(f"x_acc{n}", [P, 2, N], F32)) for n in range(X_BANKS)]

        h0_loaded, bias_loaded = sem("h0_loaded"), sem("bias_loaded")
        w_loaded = [sem(f"w_loaded{n}") for n in range(3)]
        slot_moved = [sem(f"slot_moved{n}") for n in range(RING)]
        mag_ready, mag_reduced = sem("mag_ready"), sem("mag_reduced")
        scale_step, scale_ready, unscale_ready = sem("scale_step"), sem("scale_ready"), sem("unscale_ready")
        win_hi_ready, win_lo_ready = sem("win_hi_ready"), sem("win_lo_ready")
        wrec_hi_ready, wrec_lo_ready = sem("wrec_hi_ready"), sem("wrec_lo_ready")
        ones_ready, rows_ready = sem("ones_ready"), sem("rows_ready")
        x_hi_ready, x_lo_ready = sem("x_hi_ready"), sem("x_lo_ready")
        x_group_summed, x_group_out = sem("x_group_summed"), sem("x_group_out")
        product_done = [sem(f"product_done{g}") for g in range(4)]
        part_ready = [sem(f"part_ready{g}") for g in range(4)]
        gate_summed = [sem(f"gate_summed{g}") for g in range(4)]
        gate_ready = [sem(f"gate_ready{g}") for g in range(4)]
        q_hi_ready, q_full_ready, q_lo_ready = sem("q_hi_ready"), sem("q_full_ready"), sem("q_lo_ready")
        keep_ready, new_ready = sem("keep_ready"), sem("new_ready")
        h_new_ready, h_prop_ready = sem("h_new_ready"), sem("h_prop_ready")
        h_hi_ready, h_lo_ready = sem("h_hi_ready"), sem("h_lo_ready")
        p_hi_ready, p_lo_ready = sem("p_hi_ready"), sem("p_lo_ready")
        out_unscaled, out_ready = sem("out_unscaled"), sem("out_ready")

        WEIGHTS = [(0, R), (0, Z), (0, C), (1, R), (1, Z), (1, C), (1, PROP)]

        def slot(off):
            return off % RING

        def moved(i, off):
            return 32 * (i + off // RING) + 16

        block = ctx.enter_context(nc.Block())

        @block.sync
        def _(sp):
            def load_weight(n):
                rec, g = WEIGHTS[n]
                if n >= 3:
                    was = n - 3
                    if WEIGHTS[was][0]:
                        sp.wait_ge(wrec_hi_ready, was - 2)
                        sp.wait_ge(wrec_lo_ready, was - 2)
                    else:
                        sp.wait_ge(win_hi_ready, was + 1)
                        sp.wait_ge(win_lo_ready, was + 1)
                sp.dma_start(stage[n % 3], (w_rec if rec else w_in)[g]).then_inc(w_loaded[n % 3], 16)

            def load_x(m, n):
                sp.dma_start(x_blk[n][:], x[bass.ds(m, 1)].rearrange("m p k s b -> (m p) k s b")).then_inc(slot_moved[n], 16)

            load_x(0, 0)
            load_weight(0)
            load_weight(1)
            sp.dma_start(h_prop[:], h0).then_inc(h0_loaded, 16)
            sp.dma_start(bias[:], biases).then_inc(bias_loaded, 16)
            load_weight(2)
            load_x(1, 1)
            for n in range(3, 6):
                load_weight(n)
            load_x(2, 2)
            load_weight(6)

            def store_out(m, u):
                sp.wait_ge(out_ready, CHUNK * m + CHUNK + 1)
                sp.dma_start(out[bass.ds(m, 1)].rearrange("m p k s b -> (m p) k s b"), out_blk[u][:]).then_inc(slot_moved[u], 16)

            with sp.Fori(0, (BLOCKS - RING) // RING) as i:
                for u in range(RING):
                    store_out(RING * i + u, u)
                    load_x(RING * i + u + RING, u)
            for m in range((BLOCKS - RING) // RING * RING, BLOCKS):
                store_out(m, m % RING)
                if m + RING < BLOCKS:
                    load_x(m + RING, m % RING)
            for n in range(RING):
                sp.wait_ge(slot_moved[n], 32 * len(range(n, BLOCKS, RING)))

        @block.gpsimd
        def _(pool):
            for n, col in enumerate([HS, R, Z, C, PROP]):
                pool.wait_ge(mag_ready, n + 1)
                nc.gpsimd.partition_all_reduce(mag_all[:, col:col + 1], mag[:, col:col + 1], P, ABS_MAX).then_inc(mag_reduced, 1)

            def add_x(i, off):
                u, m = slot(off), RING * i + off
                for s in range(CHUNK):
                    t = CHUNK * m + s
                    pool.wait_ge(h_new_ready, t + 1)
                    nc.gpsimd.tensor_tensor(unscaled[:], h_even_odd[s % 2][:], h_unscale_row[:], ALU.mult).then_inc(out_unscaled, 1)
                    if s == 0:
                        pool.wait_ge(slot_moved[u], moved(i, off))
                    pool.wait_ge(out_unscaled, t + 1)
                    nc.gpsimd.tensor_tensor(out_blk[u][:, :, s, :], unscaled[:], x_blk[u][:, :, s, :], ALU.add).then_inc(out_ready, 1)

            nc.gpsimd.memset(unscaled[:], 0.0).then_inc(out_ready, 1)
            pool.wait_ge(rows_ready, KC + 1)
            pool.wait_ge(out_ready, 1)
            with pool.Fori(0, LOOPS) as i:
                for u in range(RING):
                    add_x(i, u)
            for u in range(PEELED):
                add_x(LOOPS, u)

        @block.scalar
        def _(act):
            def split_x(i, off, q):
                u = slot(off)
                if q == 0:
                    act.wait_ge(slot_moved[u], moved(i, off))
                nc.scalar.copy(x_hi[u][:, q, :], x_blk[u][:, q, :, :].rearrange("p s b -> p (s b)")).then_inc(x_hi_ready, 1)

            def copy_group(i, off, n):
                m, u = RING * i + off, slot(off)
                act.wait_ge(x_group_summed, GROUPS * m + n + 1)
                g, j = divmod(n, KC)
                nc.scalar.activation(x_part[u][:, g, j, :, :].rearrange("p s b -> p (s b)"), x_acc[n % X_BANKS][:, 0, :],
                                     ACT.Identity, bias=bias[:, g, j:j + 1]).then_inc(x_group_out, 1)

            for q in range(KC):
                split_x(0, 0, q)
            for n, (rec, g) in enumerate(WEIGHTS[:GATES]):
                act.wait_ge(w_loaded[n % 3], 16)
                nc.scalar.copy(win_hi[g][:], stage[n % 3]).then_inc(win_hi_ready, 1)
            act.wait_ge(bias_loaded, 16)

            def split_rec(n):
                g = WEIGHTS[n][1]
                act.wait_ge(w_loaded[n % 3], 16 * (n // 3 + 1))
                act.wait_ge(scale_ready, n - GATES + 2)
                nc.scalar.activation(wrec_hi[g][:], stage[n % 3], ACT.Copy, scale=scale[:, g:g + 1]).then_inc(wrec_hi_ready, 1)

            for n in range(4):
                copy_group(0, 0, n)
            for q in range(KC):
                split_x(0, 1, q)
            split_rec(3)
            for n in range(4, 8):
                copy_group(0, 0, n)
            split_rec(4)
            for n in range(8, 12):
                copy_group(0, 0, n)
            split_rec(5)
            split_rec(6)

            def squash(g, func, count):
                act.wait_ge(gate_summed[g], count)
                nc.scalar.activation(gate[g][:], gate[g][:], func).then_inc(gate_ready[g], 1)

            def steps(i, off, x_next=True, x_split=True):
                m = RING * i + off
                done = issued = 0
                for s in range(CHUNK):
                    t = CHUNK * m + s
                    gaps = FILL[s]

                    def copy_finished(gap):
                        nonlocal done, issued
                        issued += gaps[gap]
                        while x_next and done < issued // PER_GROUP:
                            copy_group(i, off + 1, done)
                            done += 1

                    squash(R, ACT.Sigmoid, t + 1)
                    copy_finished(0)
                    squash(Z, ACT.Sigmoid, t + 1)
                    squash(C, ACT.Tanh, t + 1)
                    if x_split:
                        split_x(i, off + 2, s)
                    copy_finished(1)
                    if s == CHUNK - 1 and x_next:
                        squash(PROP, ACT.Tanh, m + 1)
                        copy_finished(2)

            with act.Fori(0, LOOPS) as i:
                for u in range(RING):
                    steps(i, u)
            steps(LOOPS, 0, x_split=False)
            steps(LOOPS, 1, x_next=False, x_split=False)

        @block.vector
        def _(dve):
            def flat(ap):
                return ap.rearrange("p k b -> p (k b)")

            def split_x(off, n, q):
                u = slot(off)
                dve.wait_ge(x_hi_ready, n + 1)
                nc.vector.tensor_tensor(x_lo[u][:, q, :], x_blk[u][:, q, :, :].rearrange("p s b -> p (s b)"),
                                        x_hi[u][:, q, :].bitcast(F32), ALU.subtract).then_inc(x_lo_ready, 1)

            steps_done = [0]

            def small(ins):
                steps_done[0] += 1
                ins.then_inc(scale_step, 1)
                dve.wait_ge(scale_step, steps_done[0])

            def magnitude(col, src, least):
                small(nc.vector.tensor_reduce(mag[:, col:col + 1], src, AX_X, ALU.max, apply_absolute_value=True))
                nc.vector.tensor_scalar(mag[:, col:col + 1], mag[:, col:col + 1], least, None, ALU.max).then_inc(mag_ready, 1)

            def make_scale(col, n):
                one = slice(col, col + 1)
                dve.wait_ge(mag_reduced, n)
                small(nc.vector.tensor_scalar(pow2[:, one].bitcast(U32), mag_all[:, one].bitcast(U32), EXP_MASK, None,
                                              ALU.bitwise_and))
                small(nc.vector.tensor_scalar(inv_pow2[:, one].bitcast(U32), pow2[:, one].bitcast(U32), EXP_MASK, None,
                                              ALU.bitwise_xor))
                nc.vector.tensor_scalar(scale[:, one], inv_pow2[:, one], 2.0 ** (TOP - 1), None, ALU.mult).then_inc(scale_ready, 1)
                if col == HS:
                    nc.vector.tensor_scalar(unscale[:, one], pow2[:, one], 2.0**-TOP, None, ALU.mult).then_inc(unscale_ready, 1)
                    dve.wait_ge(unscale_ready, 1)
                else:
                    nc.vector.tensor_scalar(unscale[:, one], pow2[:, one], h_unscale, 2.0**-TOP, ALU.mult,
                                            ALU.mult).then_inc(unscale_ready, 1)

            for q in range(KC):
                split_x(0, q, q)
            for n in range(GATES):
                g = WEIGHTS[n][1]
                dve.wait_ge(win_hi_ready, n + 1)
                nc.vector.tensor_tensor(win_lo[g][:], stage[n % 3], win_hi[g][:].bitcast(F32), ALU.subtract).then_inc(win_lo_ready, 1)
                if n == 1:
                    dve.wait_ge(h0_loaded, 16)
                    magnitude(HS, flat(h_prop[:]), 1.0)
            make_scale(HS, 1)
            dve.wait_ge(scale_ready, 1)
            nc.vector.tensor_scalar(h_prop[:], h_prop[:], h_scale, None, ALU.mult).then_inc(h_prop_ready, 1)
            dve.wait_ge(h_prop_ready, 1)
            nc.vector.tensor_copy(h_split[:, :, 0, :], h_prop[:]).then_inc(h_hi_ready, 1)
            dve.wait_ge(h_hi_ready, 1)
            nc.vector.tensor_tensor(h_split[:, :, 1, :], h_prop[:], h_split[:, :, 0, :], ALU.subtract).then_inc(h_lo_ready, 1)

            def split_rec(n):
                g = WEIGHTS[n][1]
                dve.wait_ge(wrec_hi_ready, n - GATES + 1)
                nc.vector.scalar_tensor_tensor(out=wrec_lo[g][:].rearrange("p k n -> p (k n)"),
                                               in0=stage[n % 3].rearrange("p k n -> p (k n)"), scalar=scale[:, g:g + 1],
                                               in1=wrec_hi[g][:].rearrange("p k n -> p (k n)"), op0=ALU.mult,
                                               op1=ALU.subtract).then_inc(wrec_lo_ready, 1)

            def rec_scale(n):
                g = WEIGHTS[n][1]
                dve.wait_ge(w_loaded[n % 3], 16 * (n // 3 + 1))
                magnitude(g, stage[n % 3].rearrange("p k n -> p (k n)"), TINY)
                make_scale(g, n - GATES + 2)

            rec_scale(3)
            split_rec(3)
            for q in range(KC):
                split_x(1, KC + q, q)
            for n in range(4, 7):
                rec_scale(n)
                split_rec(n)
            dve.wait_ge(bias_loaded, 16)
            nc.vector.memset(ones[:], 1.0).then_inc(ones_ready, 1)
            dve.wait_ge(ones_ready, 1)
            for j in range(KC):
                nc.vector.tensor_scalar(prop_bias[:, j, :], ones[:, j, :], bias[:, PROP, j:j + 1], None, ALU.mult).then_inc(rows_ready, 1)
            nc.vector.tensor_scalar(h_unscale_row[:], ones[:], h_unscale, None, ALU.mult).then_inc(rows_ready, 1)
            dve.wait_ge(rows_ready, KC + 1)

            def sum_gate(g, count, added):
                dve.wait_ge(product_done[g], count)
                nc.vector.scalar_tensor_tensor(out=part[g][:], in0=acc[g][:, :, 0, :], scalar=unscale[:, g:g + 1], in1=added,
                                               op0=ALU.mult, op1=ALU.add).then_inc(part_ready[g], 1)
                dve.wait_ge(part_ready[g], count)
                nc.vector.scalar_tensor_tensor(out=gate[g][:], in0=acc[g][:, :, 1, :], scalar=unscale[:, g:g + 1], in1=part[g][:],
                                               op0=ALU.mult, op1=ALU.add).then_inc(gate_summed[g], 1)

            def steps(i, off, last=False, x_split=True):
                m, u = RING * i + off, slot(off)
                for s in range(CHUNK):
                    t = CHUNK * m + s
                    prop = s == CHUNK - 1 and not last
                    h_in = h_prop if s == 0 else h_even_odd[(s - 1) % 2]
                    h_out = h_even_odd[s % 2]
                    if s == 0:
                        dve.wait_ge(x_group_out, GROUPS * (m + 1))
                    sum_gate(R, t + 1, x_part[u][:, R, :, s, :])

                    dve.wait_ge(gate_ready[R], t + 1)
                    nc.vector.tensor_tensor(q_split[:, :, 0, :], gate[R][:], h_in[:], ALU.mult).then_inc(q_hi_ready, 1)
                    nc.vector.tensor_tensor(q_full[:], gate[R][:], h_in[:], ALU.mult).then_inc(q_full_ready, 1)
                    dve.wait_ge(q_hi_ready, t + 1)
                    dve.wait_ge(q_full_ready, t + 1)
                    nc.vector.tensor_tensor(q_split[:, :, 1, :], q_full[:], q_split[:, :, 0, :], ALU.subtract).then_inc(q_lo_ready, 1)

                    sum_gate(Z, t + 1, x_part[u][:, Z, :, s, :])
                    sum_gate(C, t + 1, x_part[u][:, C, :, s, :])
                    dve.wait_ge(gate_ready[Z], t + 1)
                    nc.vector.scalar_tensor_tensor(out=keep[:], in0=gate[Z][:], scalar=-1.0, in1=h_in[:], op0=ALU.add,
                                                   op1=ALU.mult).then_inc(keep_ready, 1)
                    dve.wait_ge(gate_ready[C], t + 1)
                    nc.vector.scalar_tensor_tensor(out=new[:], in0=gate[C][:], scalar=h_scale, in1=gate[Z][:], op0=ALU.mult,
                                                   op1=ALU.mult).then_inc(new_ready, 1)
                    dve.wait_ge(keep_ready, t + 1)
                    dve.wait_ge(new_ready, t + 1)
                    split = p_split if prop else h_split
                    hi_ready, n_hi = (p_hi_ready, m + 1) if prop else (h_hi_ready, t + 2)
                    lo_ready = p_lo_ready if prop else h_lo_ready
                    nc.vector.tensor_tensor(split[:, :, 0, :], new[:], keep[:], ALU.subtract).then_inc(hi_ready, 1)
                    dve.wait_ge(out_ready, t + 1)
                    nc.vector.tensor_tensor(h_out[:], new[:], keep[:], ALU.subtract).then_inc(h_new_ready, 1)
                    dve.wait_ge(hi_ready, n_hi)
                    dve.wait_ge(h_new_ready, t + 1)
                    nc.vector.tensor_tensor(split[:, :, 1, :], h_out[:], split[:, :, 0, :], ALU.subtract).then_inc(lo_ready, 1)
                    if x_split:
                        split_x(off + 2, KC * (m + 2) + s, s)
                    if prop:
                        sum_gate(PROP, m + 1, prop_bias[:])
                        dve.wait_ge(gate_ready[PROP], m + 1)
                        nc.vector.tensor_scalar(h_split[:, :, 0, :], gate[PROP][:], h_scale, None, ALU.mult).then_inc(h_hi_ready, 1)
                        nc.vector.tensor_scalar(h_prop[:], gate[PROP][:], h_scale, None, ALU.mult).then_inc(h_prop_ready, 1)
                        dve.wait_ge(h_hi_ready, t + 2)
                        dve.wait_ge(h_prop_ready, m + 2)
                        nc.vector.tensor_tensor(h_split[:, :, 1, :], h_prop[:], h_split[:, :, 0, :], ALU.subtract).then_inc(h_lo_ready, 1)

            with dve.Fori(0, LOOPS) as i:
                for u in range(RING):
                    steps(i, u)
            steps(LOOPS, 0, x_split=False)
            steps(LOOPS, 1, last=True, x_split=False)

        @block.tensor
        def _(pe):
            def x_products(i, off):
                m, u = RING * i + off, slot(off)
                pe.wait_ge(x_hi_ready, KC * (m + 1))
                pe.wait_ge(x_lo_ready, KC * (m + 1))
                for n in range(GROUPS):
                    g, j = divmod(n, KC)
                    cols = slice(j * P, (j + 1) * P)
                    if not isinstance(m, int) or m * GROUPS + n >= X_BANKS:
                        pe.wait_ge(x_group_out, GROUPS * m + n + 1 - X_BANKS)
                    pairs = [(w, v, k) for k in range(KC)
                             for w, v in ((win_hi, x_hi), (win_hi, x_lo), (win_lo, x_hi))]
                    for c, (w, v, k) in enumerate(pairs):
                        mm = nc.tensor.matmul(x_acc[n % X_BANKS][:, 0, :], w[g][:, k, cols], v[u][:, k, :],
                                              start=c == 0, stop=c == PER_GROUP - 1)
                        if c == PER_GROUP - 1:
                            mm.then_inc(x_group_summed, 1)
                        yield

            def issue(products, count):
                for _ in range(count):
                    next(products)

            def recurrent(g, split, hi_ready, lo_ready, count):
                if hi_ready:
                    pe.wait_ge(hi_ready, count)
                for k in range(KC):
                    for j in range(KC):
                        nc.tensor.matmul(acc[g][:, j, 0, :], wrec_lo[g][:, k, j * P:(j + 1) * P], split[:, k, 0, :],
                                         start=k == 0 and j == 0, stop=False, skip_group_check=True)
                if lo_ready:
                    pe.wait_ge(lo_ready, count)
                for k in range(KC):
                    for j in range(KC):
                        mm = nc.tensor.matmul(acc[g][:, j, :, :].rearrange("p a b -> p (a b)"), wrec_hi[g][:, k, j * P:(j + 1) * P],
                                              split[:, k, :, :].rearrange("p a b -> p (a b)"),
                                              start=False, stop=k == KC - 1, skip_group_check=True)
                mm.then_inc(product_done[g], 1)

            first = x_products(0, 0)
            for g in range(GATES):
                pe.wait_ge(win_hi_ready, g + 1)
                pe.wait_ge(win_lo_ready, g + 1)
                issue(first, KC * PER_GROUP)
            pe.wait_ge(wrec_hi_ready, 4)
            pe.wait_ge(wrec_lo_ready, 4)

            def steps(i, off, last=False):
                m = RING * i + off
                x_next = None if last else x_products(i, off + 1)
                for s in range(CHUNK):
                    t = CHUNK * m + s
                    gaps = (0, 0, 0) if last else FILL[s]
                    recurrent(R, h_split, h_hi_ready, h_lo_ready, t + 1)
                    recurrent(Z, h_split, None, None, None)
                    issue(x_next, gaps[0])
                    recurrent(C, q_split, q_hi_ready, q_lo_ready, t + 1)
                    issue(x_next, gaps[1])
                    if s == CHUNK - 1 and not last:
                        recurrent(PROP, p_split, p_hi_ready, p_lo_ready, m + 1)
                        issue(x_next, gaps[2])

            with pe.Fori(0, LOOPS) as i:
                for u in range(RING):
                    steps(i, u)
            steps(LOOPS, 0)
            steps(LOOPS, 1, last=True)


def kernel(x, cond_1024, L0_cond_Wz, L0_cond_bz, L0_cond_Wr, L0_cond_br, L0_cond_Wh, L0_cond_bh, L0_cond_Wp, L0_cond_bp):
    import numpy as np
    import concourse.bacc as bacc
    from concourse.bass_utils import run_bass_kernel_spmd

    B, T, D = x.shape
    kc, blocks = D // P, T // CHUNK
    x = np.asarray(x)
    x_laid = x.reshape(B, blocks, CHUNK, kc, P).transpose(1, 4, 3, 2, 0)
    h0_laid = np.asarray(cond_1024).reshape(B, kc, P).transpose(2, 1, 0)
    biases = np.stack([np.asarray(b).reshape(kc, P).T for b in (L0_cond_br, L0_cond_bz, L0_cond_bh, L0_cond_bp)], axis=1)
    given = {"x": x_laid, "h0": h0_laid, "wz": L0_cond_Wz, "wr": L0_cond_Wr, "wh": L0_cond_Wh, "wp": L0_cond_Wp, "biases": biases}
    arrays = {f"{n}_dram": np.ascontiguousarray(np.asarray(a)) for n, a in given.items()}

    nc = bacc.Bacc("TRN2", target_bir_lowering=False, num_devices=1)
    args = [nc.dram_tensor(n, a.shape, mybir.dt.from_np(a.dtype), kind="ExternalInput").ap() for n, a in arrays.items()]
    out = nc.dram_tensor("out_dram", x_laid.shape, F32, kind="ExternalOutput").ap()
    gru_kernel(nc, *args, out)
    result = run_bass_kernel_spmd(nc, [arrays], core_ids=[0])
    got = result.results[0]["out_dram"]
    return np.ascontiguousarray(got.transpose(4, 0, 3, 2, 1)).reshape(B, T, D)
```

```python
from contextlib import ExitStack

import concourse.bass as bass
from concourse import mybir

ALU = mybir.AluOpType
ACT = mybir.ActivationFunctionType
F32 = mybir.dt.float32
F32R = mybir.dt.float32r
F16 = mybir.dt.float16
U32 = mybir.dt.uint32
AX_X = mybir.AxisListType.X
ABS_MAX = bass.bass_isa.ReduceOp.absmax

P = 128
CHUNK = 4
RING = 3
X_BANKS = 4
R, Z, C, PROP = range(4)
GATES = 3

EXP_MASK = 0x7F800000
TOP = 14
TINY = 2.0**-80

FILL = [(9, 0, 0, 23), (9, 0, 0, 23), (7, 0, 0, 23), (9, 22, 2, 17)]


def gru_kernel(nc, x, h0, wz, wr, wh, wp, biases, out):
    BLOCKS, _, KC, _, B = x.shape
    H = wp.shape[0]
    D = wr.shape[0] - H
    assert D == H == KC * P
    N = CHUNK * B
    GROUPS = GATES * KC
    PER_GROUP = 3 * KC
    assert sum(map(sum, FILL)) == GROUPS * PER_GROUP
    LOOPS = (BLOCKS - 2) // RING
    PEELED = BLOCKS - LOOPS * RING
    assert PEELED == 2

    rows = "(k p) n -> p k n"
    w_in = {R: wr[0:D, :].rearrange(rows, p=P), Z: wz[0:D, :].rearrange(rows, p=P), C: wh[0:D, :].rearrange(rows, p=P)}
    w_rec = {R: wr[D:, :].rearrange(rows, p=P), Z: wz[D:, :].rearrange(rows, p=P),
             C: wh[D:, :].rearrange(rows, p=P), PROP: wp.rearrange(rows, p=P)}

    with ExitStack() as ctx:
        def sb(name, shape, dt=F32):
            return ctx.enter_context(nc.sbuf_tensor(name, shape, dt))

        def sem(name):
            return ctx.enter_context(nc.semaphore(name))

        win_hi = [sb(f"win_hi{g}", [P, KC, H], F32R) for g in range(GATES)]
        win_lo = [sb(f"win_lo{g}", [P, KC, H], F32R) for g in range(GATES)]
        wrec_hi = [sb(f"wrec_hi{g}", [P, KC, H], F16) for g in range(4)]
        wrec_lo = [sb(f"wrec_lo{g}", [P, KC, H], F16) for g in range(4)]
        bias = sb("bias", [P, 4, KC])
        prop_bias = sb("prop_bias", [P, KC, B])

        x_blk = [sb(f"x_blk{n}", [P, KC, CHUNK, B]) for n in range(RING)]
        x_hi = [sb(f"x_hi{n}", [P, KC, N], F32R) for n in range(RING)]
        x_lo = [sb(f"x_lo{n}", [P, KC, N], F32R) for n in range(RING)]
        x_part = [sb(f"x_part{n}", [P, GATES, KC, CHUNK, B]) for n in range(RING)]
        STAGES = 5
        stage = [sb(f"stage{n}", [P, KC, H])[:] for n in range(STAGES - 2)] + [
            x_part[n][:, 0:2].rearrange("p g j s b -> p (g j s b)").rearrange("p (k n) -> p k n", k=KC) for n in (1, 2)]
        out_blk = [sb(f"out_blk{n}", [P, KC, CHUNK, B]) for n in range(RING)]

        HALVES = [slice(0, KC // 2), slice(KC // 2, KC)]

        h_even_odd = [sb("h_even", [P, KC, B]), sb("h_odd", [P, KC, B])]
        h_prop = sb("h_prop", [P, KC, B])
        h_split = sb("h_split", [P, KC, 2, B], F16)
        q_split = sb("q_split", [P, KC, 2, B], F16)
        p_split = q_split
        part = [sb(f"part{g}", [P, KC, B]) for g in range(GATES)]
        part.append(part[R])
        gate = [sb(f"gate{g}", [P, KC, B]) for g in range(4)]
        q_full = sb("q_full", [P, KC, B])
        keep = sb("keep", [P, KC, B])
        new = sb("new", [P, KC, B])
        unscaled = sb("unscaled", [P, KC, B])
        ones = new
        h_unscale_row = sb("h_unscale_row", [P, KC, B])

        HS = 4
        mag = sb("mag", [P, 5])
        mag_all = sb("mag_all", [P, 5])
        pow2 = sb("pow2", [P, 5])
        inv_pow2 = sb("inv_pow2", [P, 5])
        scale = sb("scale", [P, 5])
        unscale = sb("unscale", [P, 5])
        h_scale, h_unscale = scale[:, HS:HS + 1], unscale[:, HS:HS + 1]

        acc = [ctx.enter_context(nc.psum_tensor(f"acc{g}", [P, KC, 2, B], F32)) for g in range(4)]
        x_acc = [ctx.enter_context(nc.psum_tensor(f"x_acc{n}", [P, 2, N], F32)) for n in range(X_BANKS)]

        h0_loaded, bias_loaded = sem("h0_loaded"), sem("bias_loaded")
        w_loaded = [sem(f"w_loaded{n}") for n in range(STAGES)]
        slot_moved = [sem(f"slot_moved{n}") for n in range(RING)]
        mag_ready, mag_reduced = sem("mag_ready"), sem("mag_reduced")
        scale_step, scale_ready, unscale_ready = sem("scale_step"), sem("scale_ready"), sem("unscale_ready")
        win_hi_ready, win_lo_ready = sem("win_hi_ready"), [sem(f"win_lo_ready{g}") for g in range(GATES)]
        wrec_hi_ready, wrec_lo_ready = sem("wrec_hi_ready"), [sem(f"wrec_lo_ready{g}") for g in range(4)]
        prop_scaled, prop_hi_ready = sem("prop_scaled"), sem("prop_hi_ready")
        ones_ready, rows_ready = sem("ones_ready"), sem("rows_ready")
        x_hi_ready, x_lo_ready = sem("x_hi_ready"), sem("x_lo_ready")
        x_group_summed, x_group_out = sem("x_group_summed"), sem("x_group_out")
        product_done = [sem(f"product_done{g}") for g in range(4)]
        part_ready = [sem(f"part_ready{g}") for g in range(4)]
        gate_summed = [sem(f"gate_summed{g}") for g in range(4)]
        gate_ready = [sem(f"gate_ready{g}") for g in range(4)]
        q_hi_ready, q_full_ready, q_lo_ready = sem("q_hi_ready"), sem("q_full_ready"), sem("q_lo_ready")
        keep_ready, new_ready = sem("keep_ready"), sem("new_ready")
        h_new_ready, h_prop_ready = sem("h_new_ready"), sem("h_prop_ready")
        h_hi_ready, h_lo_ready = sem("h_hi_ready"), sem("h_lo_ready")
        p_hi_ready, p_lo_ready = sem("p_hi_ready"), sem("p_lo_ready")
        out_unscaled, out_ready = sem("out_unscaled"), sem("out_ready")

        C_IN = 2
        WEIGHTS = [(0, R), (0, Z), (0, C), (1, R), (1, Z), (1, C), (1, PROP)]

        def slot(off):
            return off % RING

        def moved(i, off):
            return 32 * (i + off // RING) + 16

        block = ctx.enter_context(nc.Block())

        @block.sync
        def _(sp):
            def load_weight(n):
                rec, g = WEIGHTS[n]
                if n >= STAGES:
                    assert n - STAGES < GATES - 1
                    sp.wait_ge(win_hi_ready, n - STAGES + 1)
                    sp.wait_ge(win_lo_ready[WEIGHTS[n - STAGES][1]], 1)
                sp.dma_start(stage[n % STAGES], (w_rec if rec else w_in)[g]).then_inc(w_loaded[n % STAGES], 16)

            def load_x(m, n):
                sp.dma_start(x_blk[n][:], x[bass.ds(m, 1)].rearrange("m p k s b -> (m p) k s b")).then_inc(slot_moved[n], 16)

            load_weight(0)
            load_x(0, 0)
            load_weight(1)
            sp.dma_start(h_prop[:], h0).then_inc(h0_loaded, 16)
            sp.dma_start(bias[:], biases).then_inc(bias_loaded, 16)
            for n in range(2, 5):
                load_weight(n)
            load_x(1, 1)
            load_weight(5)
            load_weight(6)
            load_x(2, 2)

            def store_out(m, u):
                sp.wait_ge(out_ready, CHUNK * m + CHUNK + 1)
                sp.dma_start(out[bass.ds(m, 1)].rearrange("m p k s b -> (m p) k s b"), out_blk[u][:]).then_inc(slot_moved[u], 16)

            with sp.Fori(0, (BLOCKS - RING) // RING) as i:
                for u in range(RING):
                    store_out(RING * i + u, u)
                    load_x(RING * i + u + RING, u)
            for m in range((BLOCKS - RING) // RING * RING, BLOCKS):
                store_out(m, m % RING)
                if m + RING < BLOCKS:
                    load_x(m + RING, m % RING)
            for n in range(RING):
                sp.wait_ge(slot_moved[n], 32 * len(range(n, BLOCKS, RING)))

        @block.gpsimd
        def _(pool):
            def split_x(off, n, q):
                u = slot(off)
                pool.wait_ge(x_hi_ready, n + 1)
                nc.gpsimd.tensor_tensor(x_lo[u][:, q, :], x_blk[u][:, q, :, :].rearrange("p s b -> p (s b)"),
                                        x_hi[u][:, q, :].bitcast(F32), ALU.subtract).then_inc(x_lo_ready, 1)

            for q in range(KC):
                split_x(0, q, q)

            def reduce_magnitude(n):
                col = [HS, R, Z, C, PROP][n]
                pool.wait_ge(mag_ready, n + 1)
                nc.gpsimd.partition_all_reduce(mag_all[:, col:col + 1], mag[:, col:col + 1], P, ABS_MAX).then_inc(mag_reduced, 1)

            reduce_magnitude(0)
            pool.wait_ge(win_hi_ready, GATES)
            for k in range(KC):
                nc.gpsimd.tensor_tensor(win_lo[C][:, k, :], stage[C_IN][:, k, :], win_hi[C][:, k, :].bitcast(F32),
                                        ALU.subtract).then_inc(win_lo_ready[C], 1)
                if k == 1:
                    reduce_magnitude(1)
            reduce_magnitude(2)
            for q in range(KC):
                split_x(1, KC + q, q)
            reduce_magnitude(3)
            reduce_magnitude(4)
            nc.gpsimd.memset(unscaled[:], 0.0).then_inc(out_ready, 1)
            pool.wait_ge(scale_ready, 5)
            prop_w = stage[(len(WEIGHTS) - 1) % STAGES]
            nc.gpsimd.tensor_scalar(prop_w, prop_w, scale[:, PROP:PROP + 1], None, ALU.mult).then_inc(prop_scaled, 1)
            pool.wait_ge(prop_scaled, 1)
            nc.gpsimd.tensor_copy(wrec_hi[PROP][:], prop_w).then_inc(prop_hi_ready, 1)
            pool.wait_ge(prop_hi_ready, 1)
            nc.gpsimd.tensor_tensor(wrec_lo[PROP][:], prop_w, wrec_hi[PROP][:], ALU.subtract).then_inc(wrec_lo_ready[PROP], 1)
            def steps(i, off, x_split=True):
                u, m = slot(off), RING * i + off
                for s in range(CHUNK):
                    t = CHUNK * m + s
                    if x_split:
                        split_x(off + 2, KC * (m + 2) + s, s)
                    pool.wait_ge(h_new_ready, 2 * t + 2)
                    nc.gpsimd.tensor_tensor(unscaled[:], h_even_odd[s % 2][:], h_unscale_row[:], ALU.mult).then_inc(out_unscaled, 1)
                    if s == 0:
                        pool.wait_ge(slot_moved[u], moved(i, off))
                    pool.wait_ge(out_unscaled, t + 1)
                    nc.gpsimd.tensor_tensor(out_blk[u][:, :, s, :], unscaled[:], x_blk[u][:, :, s, :], ALU.add).then_inc(out_ready, 1)

            pool.wait_ge(rows_ready, KC + 1)
            pool.wait_ge(out_ready, 1)
            with pool.Fori(0, LOOPS) as i:
                for u in range(RING):
                    steps(i, u)
            for u in range(PEELED):
                steps(LOOPS, u, x_split=False)

        @block.scalar
        def _(act):
            def split_x(i, off, q):
                u = slot(off)
                if q == 0:
                    act.wait_ge(slot_moved[u], moved(i, off))
                nc.scalar.copy(x_hi[u][:, q, :], x_blk[u][:, q, :, :].rearrange("p s b -> p (s b)")).then_inc(x_hi_ready, 1)

            def copy_group(i, off, n):
                m, u = RING * i + off, slot(off)
                act.wait_ge(x_group_summed, GROUPS * m + n + 1)
                g, j = divmod(n, KC)
                nc.scalar.activation(x_part[u][:, g, j, :, :].rearrange("p s b -> p (s b)"), x_acc[n % X_BANKS][:, 0, :],
                                     ACT.Identity, bias=bias[:, g, j:j + 1]).then_inc(x_group_out, 1)

            def split_in(n):
                act.wait_ge(w_loaded[n], 16)
                nc.scalar.copy(win_hi[WEIGHTS[n][1]][:], stage[n]).then_inc(win_hi_ready, 1)

            def split_rec(n):
                g = WEIGHTS[n][1]
                act.wait_ge(w_loaded[n % STAGES], 16 * (n // STAGES + 1))
                act.wait_ge(scale_ready, n - GATES + 2)
                nc.scalar.activation(wrec_hi[g][:], stage[n % STAGES], ACT.Copy, scale=scale[:, g:g + 1]).then_inc(wrec_hi_ready, 1)

            split_in(0)
            for q in range(KC):
                split_x(0, 0, q)
            split_in(1)
            split_in(2)
            act.wait_ge(bias_loaded, 16)
            for n in range(4):
                copy_group(0, 0, n)
            split_rec(3)
            for q in range(KC):
                split_x(0, 1, q)
            for n in range(4, 7):
                copy_group(0, 0, n)
            split_rec(4)
            for n in range(7, 10):
                copy_group(0, 0, n)
            split_rec(5)
            for n in range(10, GROUPS):
                copy_group(0, 0, n)
            def squash(g, func, count):
                for n, half in enumerate(HALVES):
                    act.wait_ge(gate_summed[g], count + n + 1)
                    nc.scalar.activation(gate[g][:, half, :], gate[g][:, half, :], func).then_inc(gate_ready[g], 1)

            def steps(i, off, x_next=True, x_split=True):
                m = RING * i + off
                done = issued = 0
                for s in range(CHUNK):
                    t = CHUNK * m + s
                    gaps = FILL[s]

                    def copy_finished(gap):
                        nonlocal done, issued
                        issued += gaps[gap]
                        while x_next and done < issued // PER_GROUP:
                            copy_group(i, off + 1, done)
                            done += 1

                    squash(R, ACT.Sigmoid, 2 * t)
                    act.wait_ge(gate_summed[Z], t + 1)
                    nc.scalar.activation(gate[Z][:], gate[Z][:], ACT.Sigmoid).then_inc(gate_ready[Z], 1)
                    copy_finished(0)
                    squash(C, ACT.Tanh, 2 * t)
                    if x_split:
                        split_x(i, off + 2, s)
                    if s == CHUNK - 1 and x_next:
                        copy_finished(1)
                        copy_finished(2)
                        squash(PROP, ACT.Tanh, 2 * m)
                    copy_finished(3)

            with act.Fori(0, LOOPS) as i:
                for u in range(RING):
                    steps(i, u)
            steps(LOOPS, 0, x_split=False)
            steps(LOOPS, 1, x_next=False, x_split=False)

        @block.vector
        def _(dve):
            def flat(ap):
                return ap.rearrange("p k b -> p (k b)")

            steps_done = [0]

            def small(ins):
                steps_done[0] += 1
                ins.then_inc(scale_step, 1)
                dve.wait_ge(scale_step, steps_done[0])

            def magnitude(col, src, least):
                small(nc.vector.tensor_reduce(mag[:, col:col + 1], src, AX_X, ALU.max, apply_absolute_value=True))
                nc.vector.tensor_scalar(mag[:, col:col + 1], mag[:, col:col + 1], least, None, ALU.max).then_inc(mag_ready, 1)

            def make_scale(col, n):
                one = slice(col, col + 1)
                dve.wait_ge(mag_reduced, n)
                small(nc.vector.tensor_scalar(pow2[:, one].bitcast(U32), mag_all[:, one].bitcast(U32), EXP_MASK, None,
                                              ALU.bitwise_and))
                small(nc.vector.tensor_scalar(inv_pow2[:, one].bitcast(U32), pow2[:, one].bitcast(U32), EXP_MASK, None,
                                              ALU.bitwise_xor))
                nc.vector.tensor_scalar(scale[:, one], inv_pow2[:, one], 2.0 ** (TOP - 1), None, ALU.mult).then_inc(scale_ready, 1)
                if col == HS:
                    nc.vector.tensor_scalar(unscale[:, one], pow2[:, one], 2.0**-TOP, None, ALU.mult).then_inc(unscale_ready, 1)
                    dve.wait_ge(unscale_ready, 1)
                else:
                    nc.vector.tensor_scalar(unscale[:, one], pow2[:, one], h_unscale, 2.0**-TOP, ALU.mult,
                                            ALU.mult).then_inc(unscale_ready, 1)

            def split_in(n):
                g = WEIGHTS[n][1]
                dve.wait_ge(win_hi_ready, n + 1)
                nc.vector.tensor_tensor(win_lo[g][:], stage[n], win_hi[g][:].bitcast(F32), ALU.subtract).then_inc(win_lo_ready[g], 1)

            def rec_magnitude(n):
                dve.wait_ge(w_loaded[n % STAGES], 16 * (n // STAGES + 1))
                magnitude(WEIGHTS[n][1], flat(stage[n % STAGES]), TINY)

            def split_rec(n):
                g = WEIGHTS[n][1]
                dve.wait_ge(wrec_hi_ready, n - GATES + 1)
                nc.vector.scalar_tensor_tensor(out=flat(wrec_lo[g][:]), in0=flat(stage[n % STAGES]), scalar=scale[:, g:g + 1],
                                               in1=flat(wrec_hi[g][:]), op0=ALU.mult, op1=ALU.subtract).then_inc(wrec_lo_ready[g], 1)

            split_in(0)
            dve.wait_ge(h0_loaded, 16)
            magnitude(HS, flat(h_prop[:]), 1.0)
            split_in(1)
            make_scale(HS, 1)
            rec_magnitude(3)
            dve.wait_ge(scale_ready, 1)
            for half in HALVES:
                nc.vector.tensor_scalar(h_prop[:, half, :], h_prop[:, half, :], h_scale, None, ALU.mult).then_inc(h_prop_ready, 1)
            for n, half in enumerate(HALVES):
                dve.wait_ge(h_prop_ready, n + 1)
                nc.vector.tensor_copy(h_split[:, half, 0, :], h_prop[:, half, :]).then_inc(h_hi_ready, 1)
            make_scale(R, 2)
            for n, half in enumerate(HALVES):
                dve.wait_ge(h_hi_ready, n + 1)
                nc.vector.tensor_tensor(h_split[:, half, 1, :], h_prop[:, half, :], h_split[:, half, 0, :],
                                        ALU.subtract).then_inc(h_lo_ready, 1)
            for n in range(4, 7):
                rec_magnitude(n)
                split_rec(n - 1)
                make_scale(WEIGHTS[n][1], n - GATES + 2)
            dve.wait_ge(bias_loaded, 16)
            nc.vector.memset(ones[:], 1.0).then_inc(ones_ready, 1)
            dve.wait_ge(ones_ready, 1)
            for j in range(KC):
                nc.vector.tensor_scalar(prop_bias[:, j, :], ones[:, j, :], bias[:, PROP, j:j + 1], None, ALU.mult).then_inc(rows_ready, 1)
            nc.vector.tensor_scalar(h_unscale_row[:], ones[:], h_unscale, None, ALU.mult).then_inc(rows_ready, 1)
            dve.wait_ge(rows_ready, KC + 1)

            def sum_gate(g, count, added, halves=HALVES):
                dve.wait_ge(product_done[g], count)
                before = len(halves) * (count - 1)
                for half in halves:
                    nc.vector.scalar_tensor_tensor(out=part[g][:, half, :], in0=acc[g][:, half, 0, :], scalar=unscale[:, g:g + 1],
                                                   in1=added[:, half, :], op0=ALU.mult, op1=ALU.add).then_inc(part_ready[g], 1)
                for n, half in enumerate(halves):
                    dve.wait_ge(part_ready[g], before + n + 1)
                    nc.vector.scalar_tensor_tensor(out=gate[g][:, half, :], in0=acc[g][:, half, 1, :], scalar=unscale[:, g:g + 1],
                                                   in1=part[g][:, half, :], op0=ALU.mult, op1=ALU.add).then_inc(gate_summed[g], 1)

            def low_parts(full, split, hi, whole, lo_ready):
                for n, half in enumerate(HALVES):
                    dve.wait_ge(hi[0], hi[1] + n + 1)
                    dve.wait_ge(whole[0], whole[1] + n + 1)
                    nc.vector.tensor_tensor(split[:, half, 1, :], full[:, half, :], split[:, half, 0, :],
                                            ALU.subtract).then_inc(lo_ready, 1)

            def steps(i, off, last=False):
                m, u = RING * i + off, slot(off)
                for s in range(CHUNK):
                    t = CHUNK * m + s
                    prop = s == CHUNK - 1 and not last
                    h_in = h_prop if s == 0 else h_even_odd[(s - 1) % 2]
                    h_out = h_even_odd[s % 2]
                    if s == 0:
                        dve.wait_ge(x_group_out, GROUPS * (m + 1))
                    sum_gate(R, t + 1, x_part[u][:, R, :, s, :])

                    def reset(out, half):
                        return nc.vector.tensor_tensor(out, gate[R][:, half, :], h_in[:, half, :], ALU.mult)

                    for n in range(2):
                        dve.wait_ge(gate_ready[R], 2 * t + n + 1)
                        reset(q_split[:, HALVES[n], 0, :], HALVES[n]).then_inc(q_hi_ready, 1)
                        reset(q_full[:, HALVES[n], :], HALVES[n]).then_inc(q_full_ready, 1)
                    low_parts(q_full, q_split, (q_hi_ready, 2 * t), (q_full_ready, 2 * t), q_lo_ready)

                    sum_gate(Z, t + 1, x_part[u][:, Z, :, s, :], [slice(0, KC)])
                    sum_gate(C, t + 1, x_part[u][:, C, :, s, :])
                    dve.wait_ge(gate_ready[Z], t + 1)
                    nc.vector.scalar_tensor_tensor(out=keep[:], in0=gate[Z][:], scalar=-1.0, in1=h_in[:], op0=ALU.add,
                                                   op1=ALU.mult).then_inc(keep_ready, 1)
                    for n, half in enumerate(HALVES):
                        dve.wait_ge(gate_ready[C], 2 * t + n + 1)
                        nc.vector.scalar_tensor_tensor(out=new[:, half, :], in0=gate[C][:, half, :], scalar=h_scale,
                                                       in1=gate[Z][:, half, :], op0=ALU.mult, op1=ALU.mult).then_inc(new_ready, 1)
                    dve.wait_ge(keep_ready, t + 1)
                    dve.wait_ge(out_ready, t + 1)
                    split = p_split if prop else h_split
                    hi = (p_hi_ready, 2 * m) if prop else (h_hi_ready, 2 * t + 2)
                    for n, half in enumerate(HALVES):
                        dve.wait_ge(new_ready, 2 * t + n + 1)
                        nc.vector.tensor_tensor(split[:, half, 0, :], new[:, half, :], keep[:, half, :], ALU.subtract).then_inc(hi[0], 1)
                        nc.vector.tensor_tensor(h_out[:, half, :], new[:, half, :], keep[:, half, :], ALU.subtract).then_inc(h_new_ready, 1)
                    low_parts(h_out, split, hi, (h_new_ready, 2 * t), p_lo_ready if prop else h_lo_ready)
                    if prop:
                        sum_gate(PROP, m + 1, prop_bias[:])
                        for n, half in enumerate(HALVES):
                            dve.wait_ge(gate_ready[PROP], 2 * m + n + 1)
                            nc.vector.tensor_scalar(h_split[:, half, 0, :], gate[PROP][:, half, :], h_scale, None,
                                                    ALU.mult).then_inc(h_hi_ready, 1)
                            nc.vector.tensor_scalar(h_prop[:, half, :], gate[PROP][:, half, :], h_scale, None,
                                                    ALU.mult).then_inc(h_prop_ready, 1)
                        low_parts(h_prop, h_split, (h_hi_ready, 2 * t + 2), (h_prop_ready, 2 * m + 2), h_lo_ready)

            with dve.Fori(0, LOOPS) as i:
                for u in range(RING):
                    steps(i, u)
            steps(LOOPS, 0)
            steps(LOOPS, 1, last=True)

        @block.tensor
        def _(pe):
            def x_products(i, off):
                m, u = RING * i + off, slot(off)
                pe.wait_ge(x_hi_ready, KC * (m + 1))
                pe.wait_ge(x_lo_ready, KC * (m + 1))
                for n in range(GROUPS):
                    g, j = divmod(n, KC)
                    cols = slice(j * P, (j + 1) * P)
                    if not isinstance(m, int) or m * GROUPS + n >= X_BANKS:
                        pe.wait_ge(x_group_out, GROUPS * m + n + 1 - X_BANKS)
                    pairs = [(w, v, k) for k in range(KC)
                             for w, v in ((win_hi, x_hi), (win_hi, x_lo), (win_lo, x_hi))]
                    for c, (w, v, k) in enumerate(pairs):
                        mm = nc.tensor.matmul(x_acc[n % X_BANKS][:, 0, :], w[g][:, k, cols], v[u][:, k, :],
                                              start=c == 0, stop=c == PER_GROUP - 1)
                        if c == PER_GROUP - 1:
                            mm.then_inc(x_group_summed, 1)
                        yield

            products = None

            def issue(count):
                for _ in range(count):
                    next(products)

            def low(g, split, n):
                for k in range(KC)[HALVES[n]]:
                    for j in range(KC):
                        nc.tensor.matmul(acc[g][:, j, 0, :], wrec_lo[g][:, k, j * P:(j + 1) * P], split[:, k, 0, :],
                                         start=k == 0 and j == 0, stop=False, skip_group_check=True)

            def high(g, split, chunks):
                for k in chunks:
                    for j in range(KC):
                        mm = nc.tensor.matmul(acc[g][:, j, :, :].rearrange("p a b -> p (a b)"),
                                              wrec_hi[g][:, k, j * P:(j + 1) * P],
                                              split[:, k, :, :].rearrange("p a b -> p (a b)"),
                                              start=False, stop=k == KC - 1, skip_group_check=True)
                if chunks[-1] == KC - 1:
                    mm.then_inc(product_done[g], 1)

            FIRST, SECOND = (range(KC)[half] for half in HALVES)

            products = x_products(0, 0)
            for g in range(GATES):
                pe.wait_ge(win_hi_ready, g + 1)
                pe.wait_ge(win_lo_ready[g], KC if g == C else 1)
                issue(KC * PER_GROUP)
            pe.wait_ge(wrec_hi_ready, GATES)
            for g in range(GATES):
                pe.wait_ge(wrec_lo_ready[g], 1)

            def steps(i, off, last=False):
                m = RING * i + off
                nonlocal products
                products = None if last else x_products(i, off + 1)
                for s in range(CHUNK):
                    t = CHUNK * m + s
                    gaps = (0,) * 4 if last else FILL[s]
                    pe.wait_ge(h_hi_ready, 2 * t + 1)
                    low(R, h_split, 0)
                    low(Z, h_split, 0)
                    pe.wait_ge(h_hi_ready, 2 * t + 2)
                    low(R, h_split, 1)
                    pe.wait_ge(h_lo_ready, 2 * t + 1)
                    high(R, h_split, FIRST)
                    pe.wait_ge(h_lo_ready, 2 * t + 2)
                    high(R, h_split, SECOND)
                    low(Z, h_split, 1)
                    high(Z, h_split, FIRST)
                    high(Z, h_split, SECOND[:-1])
                    issue(gaps[0])
                    pe.wait_ge(q_hi_ready, 2 * t + 1)
                    low(C, q_split, 0)
                    high(Z, h_split, SECOND[-1:])
                    pe.wait_ge(q_hi_ready, 2 * t + 2)
                    low(C, q_split, 1)
                    pe.wait_ge(q_lo_ready, 2 * t + 1)
                    high(C, q_split, FIRST)
                    pe.wait_ge(q_lo_ready, 2 * t + 2)
                    high(C, q_split, SECOND)
                    if s == CHUNK - 1 and not last:
                        issue(gaps[1])
                        pe.wait_ge(wrec_lo_ready[PROP], 1)
                        pe.wait_ge(p_hi_ready, 2 * m + 1)
                        low(PROP, p_split, 0)
                        issue(gaps[2])
                        pe.wait_ge(p_hi_ready, 2 * m + 2)
                        low(PROP, p_split, 1)
                        pe.wait_ge(p_lo_ready, 2 * m + 1)
                        high(PROP, p_split, FIRST)
                        pe.wait_ge(p_lo_ready, 2 * m + 2)
                        high(PROP, p_split, SECOND)
                    issue(gaps[3])

            with pe.Fori(0, LOOPS) as i:
                for u in range(RING):
                    steps(i, u)
            steps(LOOPS, 0)
            steps(LOOPS, 1, last=True)


def kernel(x, cond_1024, L0_cond_Wz, L0_cond_bz, L0_cond_Wr, L0_cond_br, L0_cond_Wh, L0_cond_bh, L0_cond_Wp, L0_cond_bp):
    import numpy as np
    import concourse.bacc as bacc
    from concourse.bass_utils import run_bass_kernel_spmd

    B, T, D = x.shape
    kc, blocks = D // P, T // CHUNK
    x = np.asarray(x)
    x_laid = x.reshape(B, blocks, CHUNK, kc, P).transpose(1, 4, 3, 2, 0)
    h0_laid = np.asarray(cond_1024).reshape(B, kc, P).transpose(2, 1, 0)
    biases = np.stack([np.asarray(b).reshape(kc, P).T for b in (L0_cond_br, L0_cond_bz, L0_cond_bh, L0_cond_bp)], axis=1)
    given = {"x": x_laid, "h0": h0_laid, "wz": L0_cond_Wz, "wr": L0_cond_Wr, "wh": L0_cond_Wh, "wp": L0_cond_Wp, "biases": biases}
    arrays = {f"{n}_dram": np.ascontiguousarray(np.asarray(a)) for n, a in given.items()}

    nc = bacc.Bacc("TRN2", target_bir_lowering=False, num_devices=1)
    args = [nc.dram_tensor(n, a.shape, mybir.dt.from_np(a.dtype), kind="ExternalInput").ap() for n, a in arrays.items()]
    out = nc.dram_tensor("out_dram", x_laid.shape, F32, kind="ExternalOutput").ap()
    gru_kernel(nc, *args, out)
    result = run_bass_kernel_spmd(nc, [arrays], core_ids=[0])
    got = result.results[0]["out_dram"]
    return np.ascontiguousarray(got.transpose(4, 0, 3, 2, 1)).reshape(B, T, D)
```
